# Optimizing a Trainium2 kernel written in Bass

```python
import numpy as np
import jax
import jax.numpy as jnp

def _softmax(x, axis=-1):
    return jax.nn.softmax(x, axis=axis)

def _gelu(x):
    return jax.nn.gelu(x, approximate=True)

def _silu(x):
    return jax.nn.silu(x)

def _sigmoid(x):
    return jax.nn.sigmoid(x)

def _layernorm(x, axis=-1, eps=1e-05):
    m = jnp.mean(x, axis=axis, keepdims=True)
    v = jnp.var(x, axis=axis, keepdims=True)
    return (x - m) / jnp.sqrt(v + eps)

def _scatter_add(tgt, idx, src, axis=0):
    return tgt.at[idx].add(src)

def _segment_sum(src, seg, n):
    return jax.ops.segment_sum(src, seg, n)
kernel_name = 'mk_dlrm_tower_d1_rec_r8_90793b'

def setup_inputs(seed: int=0):
    np.random.seed(seed)
    _w = jnp.asarray

    def _rec_inputs():
        import jax
        import jax.numpy as jnp
        _tk = jax.random.key(seed)
        dense_ctx = jax.random.normal(jax.random.fold_in(_tk, 190), (1024, 16), jnp.float32)
        ids = jnp.stack([jax.random.randint(jax.random.fold_in(_tk, 200 + f), (1024,), 0, v, jnp.int32) for f, v in enumerate([1250, 12500, 12500, 1250, 125000, 1250, 1000, 12500, 12500, 1250, 12500, 1250, 125000, 125000, 1000, 1000, 12500, 1000, 12500, 1000, 12500, 1000, 1250, 1000, 1250, 1250, 1000, 1000, 1250, 1000, 1000, 1000])], axis=1)
        tbl_0 = 0.05 * jax.random.normal(jax.random.fold_in(_tk, 500 + 0), (1250, 64), jnp.float32)
        tbl_1 = 0.05 * jax.random.normal(jax.random.fold_in(_tk, 500 + 1), (12500, 64), jnp.float32)
        tbl_2 = 0.05 * jax.random.normal(jax.random.fold_in(_tk, 500 + 2), (12500, 64), jnp.float32)
        tbl_3 = 0.05 * jax.random.normal(jax.random.fold_in(_tk, 500 + 3), (1250, 64), jnp.float32)
        tbl_4 = 0.05 * jax.random.normal(jax.random.fold_in(_tk, 500 + 4), (125000, 64), jnp.float32)
        tbl_5 = 0.05 * jax.random.normal(jax.random.fold_in(_tk, 500 + 5), (1250, 64), jnp.float32)
        tbl_6 = 0.05 * jax.random.normal(jax.random.fold_in(_tk, 500 + 6), (1000, 64), jnp.float32)
        tbl_7 = 0.05 * jax.random.normal(jax.random.fold_in(_tk, 500 + 7), (12500, 64), jnp.float32)
        tbl_8 = 0.05 * jax.random.normal(jax.random.fold_in(_tk, 500 + 8), (12500, 64), jnp.float32)
        tbl_9 = 0.05 * jax.random.normal(jax.random.fold_in(_tk, 500 + 9), (1250, 64), jnp.float32)
        tbl_10 = 0.05 * jax.random.normal(jax.random.fold_in(_tk, 500 + 10), (12500, 64), jnp.float32)
        tbl_11 = 0.05 * jax.random.normal(jax.random.fold_in(_tk, 500 + 11), (1250, 64), jnp.float32)
        tbl_12 = 0.05 * jax.random.normal(jax.random.fold_in(_tk, 500 + 12), (125000, 64), jnp.float32)
        tbl_13 = 0.05 * jax.random.normal(jax.random.fold_in(_tk, 500 + 13), (125000, 64), jnp.float32)
        tbl_14 = 0.05 * jax.random.normal(jax.random.fold_in(_tk, 500 + 14), (1000, 64), jnp.float32)
        tbl_15 = 0.05 * jax.random.normal(jax.random.fold_in(_tk, 500 + 15), (1000, 64), jnp.float32)
        tbl_16 = 0.05 * jax.random.normal(jax.random.fold_in(_tk, 500 + 16), (12500, 64), jnp.float32)
        tbl_17 = 0.05 * jax.random.normal(jax.random.fold_in(_tk, 500 + 17), (1000, 64), jnp.float32)
        tbl_18 = 0.05 * jax.random.normal(jax.random.fold_in(_tk, 500 + 18), (12500, 64), jnp.float32)
        tbl_19 = 0.05 * jax.random.normal(jax.random.fold_in(_tk, 500 + 19), (1000, 64), jnp.float32)
        tbl_20 = 0.05 * jax.random.normal(jax.random.fold_in(_tk, 500 + 20), (12500, 64), jnp.float32)
        tbl_21 = 0.05 * jax.random.normal(jax.random.fold_in(_tk, 500 + 21), (1000, 64), jnp.float32)
        tbl_22 = 0.05 * jax.random.normal(jax.random.fold_in(_tk, 500 + 22), (1250, 64), jnp.float32)
        tbl_23 = 0.05 * jax.random.normal(jax.random.fold_in(_tk, 500 + 23), (1000, 64), jnp.float32)
        tbl_24 = 0.05 * jax.random.normal(jax.random.fold_in(_tk, 500 + 24), (1250, 64), jnp.float32)
        tbl_25 = 0.05 * jax.random.normal(jax.random.fold_in(_tk, 500 + 25), (1250, 64), jnp.float32)
        tbl_26 = 0.05 * jax.random.normal(jax.random.fold_in(_tk, 500 + 26), (1000, 64), jnp.float32)
        tbl_27 = 0.05 * jax.random.normal(jax.random.fold_in(_tk, 500 + 27), (1000, 64), jnp.float32)
        tbl_28 = 0.05 * jax.random.normal(jax.random.fold_in(_tk, 500 + 28), (1250, 64), jnp.float32)
        tbl_29 = 0.05 * jax.random.normal(jax.random.fold_in(_tk, 500 + 29), (1000, 64), jnp.float32)
        tbl_30 = 0.05 * jax.random.normal(jax.random.fold_in(_tk, 500 + 30), (1000, 64), jnp.float32)
        tbl_31 = 0.05 * jax.random.normal(jax.random.fold_in(_tk, 500 + 31), (1000, 64), jnp.float32)
        _rk = jax.random.fold_in(_tk, 7)
        W_top1 = 0.0441942 * jax.random.normal(jax.random.fold_in(_tk, 801), (512, 512), jnp.float32)
        W_top2 = 0.0441942 * jax.random.normal(jax.random.fold_in(_tk, 802), (512, 256), jnp.float32)
        W_top3 = 0.0625 * jax.random.normal(jax.random.fold_in(_tk, 803), (256, 1), jnp.float32)
        b_top1 = jnp.zeros((512,), jnp.float32)
        b_top2 = jnp.zeros((256,), jnp.float32)
        return (dense_ctx, ids, tbl_0, tbl_1, tbl_2, tbl_3, tbl_4, tbl_5, tbl_6, tbl_7, tbl_8, tbl_9, tbl_10, tbl_11, tbl_12, tbl_13, tbl_14, tbl_15, tbl_16, tbl_17, tbl_18, tbl_19, tbl_20, tbl_21, tbl_22, tbl_23, tbl_24, tbl_25, tbl_26, tbl_27, tbl_28, tbl_29, tbl_30, tbl_31, W_top1, b_top1, W_top2, b_top2, W_top3)
    dense_ctx, ids, tbl_0, tbl_1, tbl_2, tbl_3, tbl_4, tbl_5, tbl_6, tbl_7, tbl_8, tbl_9, tbl_10, tbl_11, tbl_12, tbl_13, tbl_14, tbl_15, tbl_16, tbl_17, tbl_18, tbl_19, tbl_20, tbl_21, tbl_22, tbl_23, tbl_24, tbl_25, tbl_26, tbl_27, tbl_28, tbl_29, tbl_30, tbl_31, W_top1, b_top1, W_top2, b_top2, W_top3 = _rec_inputs()

    def _L0_rec_setup():
        import jax, jax.numpy as jnp
        import numpy as np
        BATCH = 256
        NUM_FIELDS = 32
        EMBED = 64
        NPAIRS = NUM_FIELDS * (NUM_FIELDS - 1) // 2
        ROW, COL = np.triu_indices(NUM_FIELDS, k=1)
        ROW = jnp.asarray(ROW)
        COL = jnp.asarray(COL)
        key = jax.random.key(seed)
        k1, k2 = jax.random.split(key)
        emb_inputs = jax.random.normal(k1, (BATCH, NUM_FIELDS, EMBED), dtype=jnp.float32)
        fan_in = NPAIRS * EMBED
        fan_out = EMBED * EMBED
        std = float(np.sqrt(2.0 / (fan_in + fan_out)))
        kernel = jax.random.normal(k2, (EMBED, NPAIRS, EMBED), dtype=jnp.float32) * std
        return {'emb_inputs': emb_inputs, 'kernel': kernel}
    _L0_rec_all = _L0_rec_setup()
    _L0_rec_in = {k: v for k, v in _L0_rec_all.items() if k in ('kernel',)}
    del _L0_rec_all
    return {'dense_ctx': dense_ctx, 'ids': ids, 'tbl_0': tbl_0, 'tbl_1': tbl_1, 'tbl_2': tbl_2, 'tbl_3': tbl_3, 'tbl_4': tbl_4, 'tbl_5': tbl_5, 'tbl_6': tbl_6, 'tbl_7': tbl_7, 'tbl_8': tbl_8, 'tbl_9': tbl_9, 'tbl_10': tbl_10, 'tbl_11': tbl_11, 'tbl_12': tbl_12, 'tbl_13': tbl_13, 'tbl_14': tbl_14, 'tbl_15': tbl_15, 'tbl_16': tbl_16, 'tbl_17': tbl_17, 'tbl_18': tbl_18, 'tbl_19': tbl_19, 'tbl_20': tbl_20, 'tbl_21': tbl_21, 'tbl_22': tbl_22, 'tbl_23': tbl_23, 'tbl_24': tbl_24, 'tbl_25': tbl_25, 'tbl_26': tbl_26, 'tbl_27': tbl_27, 'tbl_28': tbl_28, 'tbl_29': tbl_29, 'tbl_30': tbl_30, 'tbl_31': tbl_31, 'W_top1': W_top1, 'b_top1': b_top1, 'W_top2': W_top2, 'b_top2': b_top2, 'W_top3': W_top3, 'L0_rec_kernel': _L0_rec_in['kernel']}

def reference(dense_ctx, ids, tbl_0, tbl_1, tbl_2, tbl_3, tbl_4, tbl_5, tbl_6, tbl_7, tbl_8, tbl_9, tbl_10, tbl_11, tbl_12, tbl_13, tbl_14, tbl_15, tbl_16, tbl_17, tbl_18, tbl_19, tbl_20, tbl_21, tbl_22, tbl_23, tbl_24, tbl_25, tbl_26, tbl_27, tbl_28, tbl_29, tbl_30, tbl_31, W_top1, b_top1, W_top2, b_top2, W_top3, L0_rec_kernel):
    import jax
    import jax.numpy as jnp

    def _L0_rec_ref(emb_inputs, kernel):
        import jax, jax.numpy as jnp
        import numpy as np
        BATCH = 256
        NUM_FIELDS = 32
        EMBED = 64
        NPAIRS = NUM_FIELDS * (NUM_FIELDS - 1) // 2
        ROW, COL = np.triu_indices(NUM_FIELDS, k=1)
        ROW = jnp.asarray(ROW)
        COL = jnp.asarray(COL)
        p = emb_inputs[:, ROW]
        q = emb_inputs[:, COL]
        kp = jnp.einsum('bpj,ipj->bpi', p, kernel)
        outputs = jnp.sum(kp * q, axis=-1)
        return outputs[:, None, :]
    e = jnp.stack([tbl_0[ids[:, 0]], tbl_1[ids[:, 1]], tbl_2[ids[:, 2]], tbl_3[ids[:, 3]], tbl_4[ids[:, 4]], tbl_5[ids[:, 5]], tbl_6[ids[:, 6]], tbl_7[ids[:, 7]], tbl_8[ids[:, 8]], tbl_9[ids[:, 9]], tbl_10[ids[:, 10]], tbl_11[ids[:, 11]], tbl_12[ids[:, 12]], tbl_13[ids[:, 13]], tbl_14[ids[:, 14]], tbl_15[ids[:, 15]], tbl_16[ids[:, 16]], tbl_17[ids[:, 17]], tbl_18[ids[:, 18]], tbl_19[ids[:, 19]], tbl_20[ids[:, 20]], tbl_21[ids[:, 21]], tbl_22[ids[:, 22]], tbl_23[ids[:, 23]], tbl_24[ids[:, 24]], tbl_25[ids[:, 25]], tbl_26[ids[:, 26]], tbl_27[ids[:, 27]], tbl_28[ids[:, 28]], tbl_29[ids[:, 29]], tbl_30[ids[:, 30]], tbl_31[ids[:, 31]]], axis=1)
    z = _L0_rec_ref(e, L0_rec_kernel)
    z = z.reshape(z.shape[0], -1)
    h = jnp.concatenate([z, dense_ctx], axis=1)
    h = jnp.maximum(h @ W_top1 + b_top1, 0.0)
    h = jnp.maximum(h @ W_top2 + b_top2, 0.0)
    y = h @ W_top3
    return y

_drawn_inputs = setup_inputs


def setup_inputs(seed=0):
    import zlib

    import numpy as np

    out = dict(_drawn_inputs(seed))
    spreads = {'b_top1': (0.0, 0.1), 'b_top2': (0.0, 0.1)}
    factors = {'tbl_0': 8.0,
     'tbl_1': 8.0,
     'tbl_2': 8.0,
     'tbl_3': 8.0,
     'tbl_4': 8.0,
     'tbl_5': 8.0,
     'tbl_6': 8.0,
     'tbl_7': 8.0,
     'tbl_8': 8.0,
     'tbl_9': 8.0,
     'tbl_10': 8.0,
     'tbl_11': 8.0,
     'tbl_12': 8.0,
     'tbl_13': 8.0,
     'tbl_14': 8.0,
     'tbl_15': 8.0,
     'tbl_16': 8.0,
     'tbl_17': 8.0,
     'tbl_18': 8.0,
     'tbl_19': 8.0,
     'tbl_20': 8.0,
     'tbl_21': 8.0,
     'tbl_22': 8.0,
     'tbl_23': 8.0,
     'tbl_24': 8.0,
     'tbl_25': 8.0,
     'tbl_26': 8.0,
     'tbl_27': 8.0,
     'tbl_28': 8.0,
     'tbl_29': 8.0,
     'tbl_30': 8.0,
     'tbl_31': 8.0,
     'L0_rec_kernel': 8.0}
    for name, (base, spread) in spreads.items():
        noise = np.random.default_rng([zlib.crc32(name.encode()), seed]).standard_normal(out[name].shape)
        drawn = base * np.exp(spread * noise) if base else spread * noise
        out[name] = jnp.asarray(drawn.astype(out[name].dtype))
    for name, factor in factors.items():
        out[name] = (out[name] * factor).astype(out[name].dtype)
    return out
```

```python
import numpy as np
import concourse.bass as bass
from concourse import mybir
from contextlib import ExitStack

BATCH, FIELDS, EMBED, DENSE = 1024, 32, 64, 16
PAIRS = FIELDS * (FIELDS - 1) // 2
HID1, HID2 = 512, 256
P = 128

BB = 256
BLOCKS = BATCH // BB
SUB = BB // P
TILES = FIELDS // 2
UNITS = [(c, t) for c in range(1, FIELDS) for t in range((c + 1) // 2)]
QUAD = 4
QUADS = len(UNITS) // QUAD
ZGROUPS = 4
SLOTS = QUADS // ZGROUPS
assert len(UNITS) == 256 and SLOTS * 2 == 32

KCHUNK = 8
KCHUNKS = len(UNITS) // KCHUNK
KHALF = KCHUNK // 2 * P

NAT, HL, MOV, PROD, KST = 4, 2, 4, 4, 4
LEAD = 6
ZLAG = 2


def z_row(n, h):
    q, tile = divmod(n, QUAD)
    group, slot = divmod(q, SLOTS)
    return group, 32 * tile + 2 * slot + h


def last_quad(t):
    return ((t + 1) ** 2 - 1) // QUAD


def prep_events():
    at = {}
    for t in range(TILES):
        q = t * t // QUAD - LEAD
        at.setdefault(q % QUADS, []).append((q < 0, t))
    return at


PREP = prep_events()
AHEAD = [t for q in sorted(PREP) for nxt, t in PREP[q] if nxt]


def runs(q):
    out = []
    for k in range(QUAD):
        c, t = UNITS[QUAD * q + k]
        if out and UNITS[QUAD * q + k - 1][0] == c:
            out[-1][1] += 1
        else:
            out.append([k, 1, t])
    return out


def tower(nc, ids, tables, kern, dense, w1, b1, w2, b2, w3, out):
    f32, f32r, u32 = mybir.dt.float32, mybir.dt.float32r, mybir.dt.uint32
    ALU, ACT = mybir.AluOpType, mybir.ActivationFunctionType
    with ExitStack() as ctx:
        def sb(name, shape, dt=f32):
            return ctx.enter_context(nc.sbuf_tensor(name, shape, dt))

        def pb(name, shape):
            return ctx.enter_context(nc.psum_tensor(name, shape, f32))

        def sem(name):
            return ctx.enter_context(nc.semaphore(name))

        z_dram = nc.dram_tensor("z_dram", (ZGROUPS, P, BATCH), f32, kind="Internal").ap()

        with nc.sbuf_tensor("k_split", [P, len(UNITS) * P], f32r) as k_split:
            pass
        with ExitStack() as over:
            def sb2(name, shape):
                return over.enter_context(nc.sbuf_tensor(name, shape, f32))
            w1_sb = sb2("w1_sb", [P, ZGROUPS, HID1])
            w2_sb = sb2("w2_sb", [P, HID1 // P, HID2])
            w3_sb = sb2("w3_sb", [P, HID2 // P])
            b1_sb = sb2("b1_sb", [P, HID1 // P])
            b2_sb = sb2("b2_sb", [P, HID2 // P])
            zT = sb2("zT", [P, ZGROUPS, BATCH])
            h1T = sb2("h1T", [P, HID1 // P, BATCH])
            h2T = sb2("h2T", [P, HID2 // P, BATCH])
            y_sb = sb2("y_sb", [1, BATCH])
        ctx.enter_context(nc.sbuf_tensor("k_split_space", [P, len(UNITS) * P], f32r))

        rows = sb("rows", [P, 2, TILES, BB])
        nat = sb("nat", [P, NAT, SUB, P])
        hl = sb("hl", [P, HL, 2, BB], f32r)
        mov = sb("mov", [P, MOV, 2, 2, BB], f32r)
        prod = sb("prod", [P, PROD, QUAD, BB])
        z_sb = sb("z_sb", [P, 2, 2, BB])
        ids_sb = sb("ids_sb", [P, BATCH // P * FIELDS], u32)
        ident = sb("ident", [P, P])
        sel = sb("sel", [P, 62])

        def k_raw(s):
            return rows[:, 1, 4 * s:4 * s + 2, :].rearrange("p a b -> p (a b)")

        def k_hi(s):
            return rows[:, 1, 4 * s + 2:4 * s + 4, :].rearrange("p a b -> p (a b)").bitcast(f32r)

        u_ps = [pb(f"u_ps{s}", [P, QUAD, BB]) for s in range(2)]
        t_ps = pb("t_ps", [P, 2 * BB])
        z_ps = [pb(f"z_ps{h}", [P, 2, BB]) for h in range(2)]

        ids_in, ident_zero, ident_ready = sem("ids_in"), sem("ident_zero"), sem("ident_ready")
        sel_zero, sel_ready = sem("sel_zero"), sem("sel_ready")
        gathered = [sem(f"gathered{s}") for s in range(NAT)]
        transposed, rows_ready, hi_ready, lo_ready = sem("transposed"), sem("rows_ready"), sem("hi_ready"), sem("lo_ready")
        mov_ready = [sem(f"mov_ready{s}") for s in range(MOV)]
        k_in = [sem(f"k_in{s}") for s in range(KST)]
        k_hi_ready, k_lo_ready = sem("k_hi_ready"), sem("k_lo_ready")
        k_ready = [sem(f"k_ready{s}") for s in range(KST)]
        u_ready, prod_ready, summed = sem("u_ready"), sem("prod_ready"), sem("summed")
        z_out = sem("z_out")
        z_saved = [sem(f"z_saved{h}") for h in range(2)]
        mlp_in, z_back, dense_in = sem("mlp_in"), sem("z_back"), sem("dense_in")
        h1_ps_ready, h1_ready = sem("h1_ps_ready"), sem("h1_ready")
        h2_ps_ready, h2_ready = sem("h2_ps_ready"), sem("h2_ready")
        y_ps_ready, y_ready, stored = sem("y_ps_ready"), sem("y_ready"), sem("stored")

        def over_blocks(eng, body):
            body(0, True, False)
            with eng.Fori(1, BLOCKS - 1) as b:
                body(b, False, False)
            body(BLOCKS - 1, False, True)

        def h_ps(n):
            return u_ps[(n // 2) % 2][:, 2 * (n % 2):2 * (n % 2) + 2, :].rearrange("p a b -> p (a b)")

        block = ctx.enter_context(nc.Block())

        @block.gpsimd
        def _(pool):
            pool.wait_ge(ids_in, 16)
            for T in range(BLOCKS * TILES):
                b, t = divmod(T, TILES)
                if T >= NAT:
                    pool.wait_ge(transposed, T - NAT + 1)
                for f in (2 * t, 2 * t + 1):
                    for s in range(SUB):
                        col = (SUB * b + s) * FIELDS + f
                        pool.indirect_dma_start(
                            nat[:, T % NAT, s, (f % 2) * EMBED:(f % 2 + 1) * EMBED], None, tables[f],
                            bass.IndirectOffsetOnAxis(ids_sb[:, col:col + 1], 0)).then_inc(gathered[T % NAT], 16)
                if T == 0:
                    nc.gpsimd.memset(ident[:], 0.0).then_inc(ident_zero, 1)
                    pool.wait_ge(ident_zero, 1)
                    nc.gpsimd.affine_select(out=ident[:], in_=ident[:], compare_op=ALU.not_equal, fill=1.0, base=0,
                                            pattern=[[-1, P]], channel_multiplier=1).then_inc(ident_ready, 1)

        @block.sync
        def _(sp):
            sp.dma_start(ids_sb[:], ids).then_inc(ids_in, 16)

            def value(v):
                if not isinstance(v, int):
                    sp.compute_val(v)
                return v

            def k_load(ch):
                if ch >= KST:
                    sp.wait_ge(k_ready[ch % KST], 64 * (ch // KST))
                sp.dma_start(k_raw(ch % KST), kern[ch]).then_inc(k_in[ch % KST], 16)

            def k_spread(ch):
                s, c0 = ch % KST, ch * KCHUNK * P
                sp.wait_ge(k_lo_ready, ch + 1)
                for half in range(2):
                    cols = slice(c0 + half * KHALF, c0 + (half + 1) * KHALF)
                    src = slice(EMBED * half, EMBED * (half + 1))
                    sp.dma_start(k_split[0:EMBED, cols].bitcast(f32), k_hi(s)[src, :].bitcast(f32)).then_inc(k_ready[s], 16)
                    sp.dma_start(k_split[EMBED:P, cols].bitcast(f32), k_raw(s)[src, :]).then_inc(k_ready[s], 16)

            def mov_spread(b, t):
                old = t - MOV
                split = value(b * TILES + t + 1)
                if old >= 0:
                    used = value(b * QUADS + last_quad(old) + 1)
                elif not (isinstance(b, int) and b == 0):
                    used = value((b - 1) * QUADS + last_quad(old + TILES) + 1)
                else:
                    used = 0
                sp.wait_ge(lo_ready, split)
                if not (isinstance(used, int) and used == 0):
                    sp.wait_ge(u_ready, used)
                for f in range(2):
                    for half in range(2):
                        sp.dma_start(mov[EMBED * half:EMBED * (half + 1), t % MOV, f].bitcast(f32),
                                     hl[EMBED * f:EMBED * (f + 1), t % HL].bitcast(f32)).then_inc(mov_ready[t % MOV], 16)

            for ch in range(KST):
                k_load(ch)
            ch_next = 0
            for t in AHEAD:
                k_spread(ch_next)
                if ch_next >= 2:
                    k_load(ch_next + 2)
                ch_next += 1
                mov_spread(0, t)

            def body(b, first, last):
                ch = ch_next
                for q in range(QUADS):
                    for nxt, t in PREP.get(q, []):
                        if not (nxt and last):
                            mov_spread(b + 1 if nxt else b, t)
                    if first and q % 2 == 0 and ch < KCHUNKS:
                        k_spread(ch)
                        if ch + 2 < KCHUNKS:
                            k_load(ch + 2)
                        ch += 1

            over_blocks(sp, body)

            sp.wait_ge(u_ready, BLOCKS * QUADS)
            sp.dma_start(w1_sb[:], w1).then_inc(mlp_in, 16)
            sp.dma_start(w2_sb[:], w2).then_inc(mlp_in, 16)
            sp.dma_start(w3_sb[:], w3).then_inc(mlp_in, 16)
            sp.dma_start(b1_sb[:], b1).then_inc(mlp_in, 16)
            sp.dma_start(b2_sb[:], b2).then_inc(mlp_in, 16)
            for h in range(2):
                sp.wait_ge(z_saved[h], 16 * BLOCKS)
            sp.dma_start(zT[:], z_dram.rearrange("g p n -> p g n")).then_inc(z_back, 16)
            sp.wait_ge(z_back, 16)
            k = 0
            for n, (c, t) in enumerate(UNITS):
                if c == 2 * t + 1:
                    g, r = z_row(n, 1)
                    sp.dma_start(zT[r:r + 1, g, :], dense[k:k + 1, :]).then_inc(dense_in, 16)
                    k += 1
            sp.wait_ge(y_ready, 2)
            sp.dma_start(out, y_sb[:]).then_inc(stored, 16)
            sp.wait_ge(stored, 16)

        @block.scalar
        def _(act):
            def k_round(ch):
                s = ch % KST
                act.wait_ge(k_in[s], 16 * (ch // KST + 1))
                nc.scalar.activation(k_hi(s), k_raw(s), ACT.Copy).then_inc(k_hi_ready, 1)

            def rows_out(b, t):
                act.wait_ge(transposed, b * TILES + t + 1)
                if not (isinstance(b, int) and b == 0):
                    if t == 0 and isinstance(b, int) and b == 1:
                        for s in range(KST):
                            act.wait_ge(k_ready[s], 64 * (KCHUNKS // KST))
                    if isinstance(b, int) and b == 1:
                        pass
                    elif t == 0:
                        act.wait_ge(prod_ready, (b - 1) * QUADS)
                nc.scalar.activation(rows[:, b % 2, t, :], t_ps[:, 0:BB], ACT.Copy).then_inc(rows_ready, 1)
                use = t - HL
                if use >= 0:
                    act.wait_ge(mov_ready[use % MOV], 64 * (b * (TILES // MOV) + use // MOV + 1))
                elif not (isinstance(b, int) and b == 0):
                    act.wait_ge(mov_ready[use % MOV], 64 * b * (TILES // MOV))
                nc.scalar.activation(hl[:, t % HL, 0, :], t_ps[:, 0:BB], ACT.Copy).then_inc(hi_ready, 1)

            def z_evacuate(b, h):
                act.wait_ge(summed, b * QUADS + (h + 1) * (QUADS // 2))
                if not (isinstance(b, int) and b == 0):
                    act.wait_ge(z_saved[h], 16 * b)
                nc.scalar.activation(z_sb[:, h], z_ps[h][:], ACT.Copy).then_inc(z_out, 1)
                act.wait_ge(z_out, 2 * b + h + 1)
                act.dma_start(z_dram[2 * h:2 * h + 2, :, bass.ds(b * BB, BB)].rearrange("g p n -> p g n"),
                              z_sb[:, h]).then_inc(z_saved[h], 16)

            for ch in range(2):
                k_round(ch)
            ch0 = 2
            for t in AHEAD:
                rows_out(0, t)
                k_round(ch0)
                ch0 += 1

            def body(b, first, last):
                ch = ch0
                for q in range(QUADS):
                    if q == ZLAG + 1 and not first:
                        z_evacuate(b - 1, 1)
                    if q == QUADS // 2 + ZLAG + 1:
                        z_evacuate(b, 0)
                    for nxt, t in PREP.get(q, []):
                        if not (nxt and last):
                            rows_out(b + 1 if nxt else b, t)
                    if first and q % 2 == 0 and ch < KCHUNKS:
                        k_round(ch)
                        ch += 1

            body(0, True, False)
            with act.Fori(1, BLOCKS - 1) as b:
                body(b, False, False)
            body(BLOCKS - 1, False, True)
            z_evacuate(BLOCKS - 1, 1)

            act.wait_ge(mlp_in, 80)
            n = 0
            for hb in range(2):
                cols = slice(hb * 512, (hb + 1) * 512)
                for m in range(HID1 // P):
                    n += 1
                    act.wait_ge(h1_ps_ready, n)
                    nc.scalar.activation(h1T[:, m, cols], h_ps(n - 1), ACT.Relu, bias=b1_sb[:, m:m + 1]).then_inc(h1_ready, 1)
            for hb in range(2):
                cols = slice(hb * 512, (hb + 1) * 512)
                for m in range(HID2 // P):
                    n += 1
                    act.wait_ge(h2_ps_ready, n - 8)
                    nc.scalar.activation(h2T[:, m, cols], h_ps(n - 1), ACT.Relu, bias=b2_sb[:, m:m + 1]).then_inc(h2_ready, 1)
            for hb in range(2):
                act.wait_ge(y_ps_ready, hb + 1)
                nc.scalar.activation(y_sb[0:1, hb * 512:(hb + 1) * 512], h_ps(n)[0:1, :], ACT.Copy).then_inc(y_ready, 1)
                n += 1

        @block.vector
        def _(dve):
            nc.vector.memset(sel[:], 0.0).then_inc(sel_zero, 1)
            dve.wait_ge(sel_zero, 1)
            nc.vector.memset(sel[0:EMBED, 30:31], 1.0).then_inc(sel_ready, 1)
            nc.vector.memset(sel[EMBED:P, 31:32], 1.0).then_inc(sel_ready, 1)

            def k_rest(ch):
                dve.wait_ge(k_hi_ready, ch + 1)
                s = ch % KST
                nc.vector.tensor_tensor(k_raw(s).bitcast(f32r), k_raw(s), k_hi(s), ALU.subtract).then_inc(k_lo_ready, 1)

            def rows_rest(b, t):
                dve.wait_ge(rows_ready, b * TILES + t + 1)
                dve.wait_ge(hi_ready, b * TILES + t + 1)
                nc.vector.tensor_tensor(hl[:, t % HL, 1, :], rows[:, b % 2, t, :], hl[:, t % HL, 0, :],
                                        ALU.subtract).then_inc(lo_ready, 1)

            for ch in range(2):
                k_rest(ch)
            ch0 = 2
            for t in AHEAD:
                rows_rest(0, t)
                k_rest(ch0)
                ch0 += 1

            def body(b, first, last):
                ch = ch0
                for q in range(QUADS):
                    for nxt, t in PREP.get(q, []):
                        if not (nxt and last):
                            rows_rest(b + 1 if nxt else b, t)
                    if first and q % 2 == 0 and ch < KCHUNKS:
                        k_rest(ch)
                        ch += 1
                    dve.wait_ge(u_ready, b * QUADS + q + 1)
                    if not first or q >= PROD:
                        dve.wait_ge(summed, b * QUADS + q - PROD + 1)
                    for k, count, t in runs(q):
                        op = nc.vector.tensor_tensor(prod[:, q % PROD, k:k + count, :], u_ps[q % 2][:, k:k + count, :],
                                                     rows[:, b % 2, t:t + count, :], ALU.mult)
                    op.then_inc(prod_ready, 1)

            over_blocks(dve, body)

        @block.tensor
        def _(pe):
            def transpose(b, t):
                pe.wait_ge(gathered[t % NAT], 64 * (b * (TILES // NAT) + t // NAT + 1))
                if not (isinstance(b, int) and b == 0 and t == 0):
                    pe.wait_ge(hi_ready, b * TILES + t)
                for s in range(SUB):
                    op = nc.tensor.transpose(t_ps[:, s * P:(s + 1) * P], nat[:, t % NAT, s, :], ident[:])
                op.then_inc(transposed, 1)

            def interact(b, q, first):
                if not first or q >= 2:
                    pe.wait_ge(prod_ready, b * QUADS + q - 1)
                if first and q % (KCHUNK // QUAD) == 0:
                    ch = q // (KCHUNK // QUAD)
                    pe.wait_ge(k_ready[ch % KST], 64 * (ch // KST + 1))
                for k in range(QUAD):
                    n = QUAD * q + k
                    c, t = UNITS[n]
                    ct = c // 2
                    if t == 0:
                        pe.wait_ge(mov_ready[ct % MOV], 64 * (b * (TILES // MOV) + ct // MOV + 1))
                    for part in range(2):
                        op = nc.tensor.matmul(u_ps[q % 2][:, k, :], k_split[:, n * P:(n + 1) * P],
                                              mov[:, ct % MOV, c % 2, part, :], start=part == 0, stop=part == 1)
                op.then_inc(u_ready, 1)

            def add_up(b, q):
                group, slot = divmod(q, SLOTS)
                pe.wait_ge(prod_ready, b * QUADS + q + 1)
                if q % (QUADS // 2) == 0 and not (isinstance(b, int) and b == 0):
                    pe.wait_ge(z_out, 2 * (b - 1) + q // (QUADS // 2) + 1)
                for k in range(QUAD):
                    op = nc.tensor.matmul(z_ps[group // 2][32 * k:32 * k + 32, group % 2, :],
                                          sel[:, 30 - 2 * slot:62 - 2 * slot], prod[:, q % PROD, k, :],
                                          start=slot == 0, stop=slot == SLOTS - 1)
                op.then_inc(summed, 1)

            pe.wait_ge(ident_ready, 1)
            pe.wait_ge(sel_ready, 2)
            for t in AHEAD:
                transpose(0, t)

            def body(b, first, last):
                for q in range(QUADS):
                    for nxt, t in PREP.get(q, []):
                        if not (nxt and last):
                            transpose(b + 1 if nxt else b, t)
                    interact(b, q, first)
                    if q >= ZLAG:
                        add_up(b, q - ZLAG)
                    elif not first:
                        add_up(b - 1, q - ZLAG + QUADS)

            over_blocks(pe, body)
            for q in range(QUADS - ZLAG, QUADS):
                add_up(BLOCKS - 1, q)

            pe.wait_ge(prod_ready, BLOCKS * QUADS)
            pe.wait_ge(mlp_in, 80)
            pe.wait_ge(z_back, 16)
            pe.wait_ge(dense_in, 16 * DENSE)
            n = 0
            for hb in range(2):
                cols = slice(hb * 512, (hb + 1) * 512)
                for m in range(HID1 // P):
                    if n >= 4:
                        pe.wait_ge(h1_ready, n - 3)
                    for g in range(ZGROUPS):
                        op = nc.tensor.matmul(h_ps(n), w1_sb[:, g, m * P:(m + 1) * P], zT[:, g, cols],
                                              start=g == 0, stop=g == ZGROUPS - 1)
                    op.then_inc(h1_ps_ready, 1)
                    n += 1
            for hb in range(2):
                cols = slice(hb * 512, (hb + 1) * 512)
                pe.wait_ge(h1_ready, 4 * (hb + 1))
                for m in range(HID2 // P):
                    pe.wait_ge(h1_ready, n - 3)
                    for g in range(HID1 // P):
                        op = nc.tensor.matmul(h_ps(n), w2_sb[:, g, m * P:(m + 1) * P], h1T[:, g, cols],
                                              start=g == 0, stop=g == HID1 // P - 1)
                    op.then_inc(h2_ps_ready, 1)
                    n += 1
            for hb in range(2):
                cols = slice(hb * 512, (hb + 1) * 512)
                pe.wait_ge(h2_ready, 2 * (hb + 1))
                for g in range(HID2 // P):
                    op = nc.tensor.matmul(h_ps(n)[0:1, :], w3_sb[:, g:g + 1], h2T[:, g, cols],
                                          start=g == 0, stop=g == HID2 // P - 1)
                op.then_inc(y_ps_ready, 1)
                n += 1


def kernel(**inputs):
    import concourse.bacc as bacc
    from concourse.bass_utils import run_bass_kernel_spmd

    nc = bacc.Bacc("TRN2", target_bir_lowering=False, num_devices=1)
    arrays = {}

    def dram(name, a):
        a = np.ascontiguousarray(a)
        arrays[name] = a
        return nc.dram_tensor(name, a.shape, mybir.dt.from_np(a.dtype), kind="ExternalInput").ap()

    k_in = np.asarray(inputs["L0_rec_kernel"])
    w1_in = np.asarray(inputs["W_top1"])
    first = [r * (2 * FIELDS - r - 1) // 2 - r - 1 for r in range(FIELDS)]
    k_units = np.zeros((EMBED, len(UNITS), 2, EMBED), k_in.dtype)
    w1_rows = np.zeros((ZGROUPS, P, HID1), w1_in.dtype)
    spare = 0
    for n, (c, t) in enumerate(UNITS):
        for h in range(2):
            r = 2 * t + h
            if r < c:
                k_units[:, n, h] = k_in[:, first[r] + c]
                w1_rows[z_row(n, h)] = w1_in[first[r] + c]
            else:
                w1_rows[z_row(n, h)] = w1_in[PAIRS + spare]
                spare += 1
    kern = k_units.reshape(EMBED, KCHUNKS, 2, KHALF).transpose(1, 2, 0, 3).reshape(KCHUNKS, P, KHALF)
    ids = np.asarray(inputs["ids"]).reshape(BATCH // P, P, FIELDS).transpose(1, 0, 2).reshape(P, -1).view(np.uint32)

    args = [dram("ids", ids), [dram(f"tbl_{f}", np.asarray(inputs[f"tbl_{f}"])) for f in range(FIELDS)],
            dram("kern", kern), dram("dense", np.asarray(inputs["dense_ctx"]).T),
            dram("w1", w1_rows.transpose(1, 0, 2)), dram("b1", np.asarray(inputs["b_top1"]).reshape(-1, P).T),
            dram("w2", np.asarray(inputs["W_top2"]).reshape(-1, P, HID2).transpose(1, 0, 2)),
            dram("b2", np.asarray(inputs["b_top2"]).reshape(-1, P).T),
            dram("w3", np.asarray(inputs["W_top3"]).reshape(-1, P).T)]
    out = nc.dram_tensor("out", (1, BATCH), mybir.dt.float32, kind="ExternalOutput").ap()
    tower(nc, *args, out)
    r = run_bass_kernel_spmd(nc, [arrays], core_ids=[0])
    return r.results[0]["out"].reshape(BATCH, 1)
```

```python
import numpy as np
import concourse.bass as bass
from concourse import mybir
from contextlib import ExitStack

BATCH, FIELDS, EMBED, DENSE = 1024, 32, 64, 16
PAIRS = FIELDS * (FIELDS - 1) // 2
HID1, HID2 = 512, 256
P = 128

BB = 256
BLOCKS = BATCH // BB
SUB = BB // P
TILES = FIELDS // 2
UNITS = [(c, t) for c in range(1, FIELDS) for t in range((c + 1) // 2)]
QUAD = 4
QUADS = len(UNITS) // QUAD
ZGROUPS = 4
SLOTS = QUADS // ZGROUPS
assert len(UNITS) == 256 and SLOTS * 2 == 32

KCHUNK = 8
KCHUNKS = len(UNITS) // KCHUNK
KCOLS = KCHUNK * P
KAHEAD = 5

NAT, HL, MOV, PROD, KST = 4, 4, 4, 4, 4
LEAD = 7
ZLAG = 2


def z_row(n, h):
    q, tile = divmod(n, QUAD)
    group, slot = divmod(q, SLOTS)
    return group, 32 * tile + 2 * slot + h


def last_quad(t):
    return ((t + 1) ** 2 - 1) // QUAD


def first_quad(t):
    return t * t // QUAD if t else -1


SPLIT_AT = [first_quad(t) - LEAD for t in range(TILES)]
REST_AT = [q + 1 for q in SPLIT_AT]
SPREAD_AT = [max(SPLIT_AT[t] + 2, last_quad((t - MOV) % TILES) - (QUADS if t < MOV else 0) + 1) for t in range(TILES)]
assert all(SPREAD_AT[t] <= first_quad(t) for t in range(1, TILES)) and SPREAD_AT == sorted(SPREAD_AT)
assert all(SPREAD_AT[(t - HL) % TILES] - (QUADS if t < HL else 0) < SPLIT_AT[t] for t in range(TILES))


def events(at):
    out = {}
    for t, q in enumerate(at):
        out.setdefault(q % QUADS, []).append((q < 0, t))
    return out


SPLIT, REST, SPREAD = events(SPLIT_AT), events(REST_AT), events(SPREAD_AT)
AHEAD = range(min(SPLIT_AT), 0)


SPARE_ROWS = [z_row(n, 1) for n, (c, t) in enumerate(UNITS) if c == 2 * t + 1]
assert len(SPARE_ROWS) == DENSE

W1_SPLIT = {28: 0, 31: 1, 34: 2, 37: 3}
W2_SPLIT = {40: 0}
Z_SPLIT = {45: 0, 48: 1, 51: 2, 54: 3}
Z_LAST_SPLIT = {58: 0, 60: 1}


def runs(q):
    out = []
    for k in range(QUAD):
        c, t = UNITS[QUAD * q + k]
        if out and UNITS[QUAD * q + k - 1][0] == c:
            out[-1][1] += 1
        else:
            out.append([k, 1, t])
    return out


def tower(nc, ids, tables, kern, dense, w1, b1, w2, b2, w3, out):
    f32, f32r, u32 = mybir.dt.float32, mybir.dt.float32r, mybir.dt.uint32
    ALU, ACT = mybir.AluOpType, mybir.ActivationFunctionType
    with ExitStack() as ctx:
        def sb(name, shape, dt=f32):
            return ctx.enter_context(nc.sbuf_tensor(name, shape, dt))

        def pb(name, shape):
            return ctx.enter_context(nc.psum_tensor(name, shape, f32))

        def sem(name):
            return ctx.enter_context(nc.semaphore(name))

        z_dram = nc.dram_tensor("z_dram", (ZGROUPS, P, BATCH), f32, kind="Internal").ap()

        with nc.sbuf_tensor("k_split", [P, len(UNITS) * P], f32r) as k_split:
            pass
        over, over_bytes = ExitStack(), [0]
        with over:
            def sb2(name, shape, dt=f32):
                over_bytes[0] += 4 * int(np.prod(shape[1:]))
                return (over.enter_context(nc.sbuf_tensor(name, shape, dt)),
                        min(QUADS, -(-over_bytes[0] // (4 * P * QUAD))))
            w1_sb, _ = sb2("w1_sb", [P, ZGROUPS, HID1])
            w2_sb, _ = sb2("w2_sb", [P, HID1 // P, HID2])
            zT, mlp_raw_quads = sb2("zT", [P, ZGROUPS, BATCH])
            w1_hl, _ = sb2("w1_hl", [P, 2, ZGROUPS, HID1], f32r)
            w2_hl, w_quads = sb2("w2_hl", [P, 2, HID1 // P, HID2], f32r)
            z_hl, z_quads = sb2("z_hl", [P, 2, ZGROUPS, BATCH], f32r)
            h1_hl, _ = sb2("h1_hl", [P, 2, HID1 // P, BATCH], f32r)
            h2T, _ = sb2("h2T", [P, HID2 // P, BATCH])
            y_sb, _ = sb2("y_sb", [1, BATCH])
        assert over_bytes[0] <= 4 * P * len(UNITS)
        ctx.enter_context(nc.sbuf_tensor("k_split_space", [P, len(UNITS) * P], f32r))

        rows = sb("rows", [P, 2, TILES, BB])
        nat = sb("nat", [P, NAT, SUB, P])
        hl = sb("hl", [P, HL, 2, BB], f32r)
        mov = sb("mov", [P, MOV, 2, 2, BB], f32r)
        prod = sb("prod", [P, PROD, QUAD, BB])
        z_sb = sb("z_sb", [P, 2, BB])
        ids_sb = sb("ids_sb", [P, BATCH // P * FIELDS], u32)
        ident = sb("ident", [P, P])
        sel = sb("sel", [P, 62])
        w3_sb = sb("w3_sb", [P, HID2 // P])
        b1_sb = sb("b1_sb", [P, HID1 // P])
        b2_sb = sb("b2_sb", [P, HID2 // P])

        def k_raw(s):
            return rows[:, 1, 4 * s:4 * s + 4, :].rearrange("p a b -> p (a b)")

        def h1_raw(n):
            return w1_sb[:, n % 4, :]

        u_ps = [pb(f"u_ps{s}", [P, QUAD, BB]) for s in range(2)]
        t_ps = pb("t_ps", [P, BB])
        z_ps = [pb(f"z_ps{h}", [P, 2, BB]) for h in range(2)]

        ids_in, ident_zero, ident_ready = sem("ids_in"), sem("ident_zero"), sem("ident_ready")
        sel_zero, sel_ready = sem("sel_zero"), sem("sel_ready")
        gathered = [sem(f"gathered{s}") for s in range(NAT)]
        transposed, rows_ready, lo_ready, mov_ready = sem("transposed"), sem("rows_ready"), sem("lo_ready"), sem("mov_ready")
        k_in = [sem(f"k_in{s}") for s in range(KST)]
        k_hi_ready, k_ready = sem("k_hi_ready"), sem("k_ready")
        u_ready, prod_ready, summed = sem("u_ready"), sem("prod_ready"), sem("summed")
        z_out = sem("z_out")
        z_saved = sem("z_saved")
        small_in, w_in, z_back = sem("small_in"), sem("w_in"), sem("z_back")
        z_last_out = sem("z_last_out")
        dense_in = [sem(f"dense_in{n}") for n in range(3)]
        w_hi_ready, w_ready, zs_hi_ready, z_ready = sem("w_hi_ready"), sem("w_ready"), sem("zs_hi_ready"), sem("z_ready")
        h1_ps_ready, h1_relu, h1_hi_ready, h1_ready = sem("h1_ps_ready"), sem("h1_relu"), sem("h1_hi_ready"), sem("h1_ready")
        h2_ps_ready, h2_ready = sem("h2_ps_ready"), sem("h2_ready")
        y_ps_ready, y_ready, stored = sem("y_ps_ready"), sem("y_ready"), sem("stored")

        def over_blocks(eng, body):
            body(0, True, False)
            with eng.Fori(1, BLOCKS - 1) as b:
                body(b, False, False)
            body(BLOCKS - 1, False, True)

        def h_ps(n):
            return u_ps[(n // 2) % 2][:, 2 * (n % 2):2 * (n % 2) + 2, :].rearrange("p a b -> p (a b)")

        block = ctx.enter_context(nc.Block())

        @block.gpsimd
        def _(pool):
            pool.wait_ge(ids_in, 16)
            for T in range(BLOCKS * TILES):
                b, t = divmod(T, TILES)
                if T >= NAT:
                    pool.wait_ge(transposed, T - NAT + 1)
                for f in (2 * t, 2 * t + 1):
                    for s in range(SUB):
                        col = (SUB * b + s) * FIELDS + f
                        pool.indirect_dma_start(
                            nat[:, T % NAT, s, (f % 2) * EMBED:(f % 2 + 1) * EMBED], None, tables[f],
                            bass.IndirectOffsetOnAxis(ids_sb[:, col:col + 1], 0)).then_inc(gathered[T % NAT], 16)
                if T == 0:
                    nc.gpsimd.memset(ident[:], 0.0).then_inc(ident_zero, 1)
                    pool.wait_ge(ident_zero, 1)
                    nc.gpsimd.affine_select(out=ident[:], in_=ident[:], compare_op=ALU.not_equal, fill=1.0, base=0,
                                            pattern=[[-1, P]], channel_multiplier=1).then_inc(ident_ready, 1)

        @block.sync
        def _(sp):
            sp.dma_start(ids_sb[:], ids).then_inc(ids_in, 16)
            for ch in range(KCHUNKS):
                if ch >= KST:
                    sp.wait_ge(k_ready, ch - KST + 1)
                for half in range(2):
                    sp.dma_start(k_raw(ch % KST)[EMBED * half:EMBED * (half + 1), :], kern[ch]).then_inc(k_in[ch % KST], 16)
            sp.dma_start(w3_sb[:], w3).then_inc(small_in, 16)
            sp.dma_start(b1_sb[:], b1).then_inc(small_in, 16)
            sp.dma_start(b2_sb[:], b2).then_inc(small_in, 16)

            done = (BLOCKS - 1) * BB
            sp.wait_ge(u_ready, (BLOCKS - 1) * QUADS + mlp_raw_quads)
            sp.dma_start(w1_sb[:], w1).then_inc(w_in, 16)
            sp.dma_start(w2_sb[:], w2).then_inc(w_in, 16)
            sp.wait_ge(z_saved, 32 * (BLOCKS - 1))
            sp.dma_start(zT[:, :, 0:done], z_dram[:, :, 0:done].rearrange("g p n -> p g n")).then_inc(z_back, 16)

            def dense_rows(groups, cols, landed):
                for k, (g, r) in enumerate(SPARE_ROWS):
                    if g in groups:
                        sp.dma_start(zT[r:r + 1, g, cols], dense[k:k + 1, cols]).then_inc(landed, 16)

            sp.wait_ge(z_back, 16)
            dense_rows((0, 1, 2, 3), slice(0, done), dense_in[0])
            for h in range(2):
                sp.wait_ge(z_last_out, h + 1)
                dense_rows((2 * h, 2 * h + 1), slice(done, BATCH), dense_in[1 + h])
            sp.wait_ge(y_ready, 2)
            sp.dma_start(out, y_sb[:]).then_inc(stored, 16)
            sp.wait_ge(stored, 16)

        @block.scalar
        def _(act):
            def k_round(ch):
                act.wait_ge(k_in[ch % KST], 32 * (ch // KST + 1))
                nc.scalar.activation(k_split[:, ch * KCOLS:(ch + 1) * KCOLS], k_raw(ch % KST), ACT.Copy).then_inc(k_hi_ready, 1)

            def split_tile(b, t):
                first, second = isinstance(b, int) and b == 0, isinstance(b, int) and b == 1
                act.wait_ge(transposed, b * TILES + t + 1)
                nc.scalar.activation(hl[:, t % HL, 0, :], t_ps[:], ACT.Copy)
                if t == 0 and second:
                    act.wait_ge(k_ready, KCHUNKS)
                elif t == 0 and not first:
                    act.wait_ge(prod_ready, (b - 1) * QUADS)
                nc.scalar.activation(rows[:, b % 2, t, :], t_ps[:], ACT.Copy).then_inc(rows_ready, 1)

            def spread_tile(b, t):
                act.wait_ge(lo_ready, b * TILES + t + 1)
                if t >= MOV:
                    act.wait_ge(u_ready, b * QUADS + last_quad(t - MOV) + 1)
                elif not (isinstance(b, int) and b == 0):
                    act.wait_ge(u_ready, (b - 1) * QUADS + last_quad(t - MOV + TILES) + 1)
                for f in range(2):
                    for half in range(2):
                        op = nc.scalar.activation(mov[EMBED * half:EMBED * (half + 1), t % MOV, f],
                                                  hl[EMBED * f:EMBED * (f + 1), t % HL], ACT.Copy)
                op.then_inc(mov_ready, 1)

            def z_evacuate(b, h):
                act.wait_ge(summed, b * QUADS + (h + 1) * (QUADS // 2))
                if not (isinstance(b, int) and b == 0 and h == 0):
                    act.wait_ge(z_saved, 32 * b + 16 * h)
                nc.scalar.activation(z_sb[:], z_ps[h][:], ACT.Copy).then_inc(z_out, 1)
                act.wait_ge(z_out, 2 * b + h + 1)
                act.dma_start(z_dram[2 * h:2 * h + 2, :, bass.ds(b * BB, BB)].rearrange("g p n -> p g n"),
                              z_sb[:]).then_inc(z_saved, 16)

            def z_evacuate_last(h):
                act.wait_ge(summed, (BLOCKS - 1) * QUADS + (h + 1) * (QUADS // 2))
                nc.scalar.activation(zT[:, 2 * h:2 * h + 2, (BLOCKS - 1) * BB:], z_ps[h][:], ACT.Copy).then_inc(z_last_out, 1)

            def mlp_round(q):
                if q in W1_SPLIT:
                    g = W1_SPLIT[q]
                    if g == 0:
                        act.wait_ge(w_in, 32)
                        act.wait_ge(u_ready, (BLOCKS - 1) * QUADS + w_quads)
                    nc.scalar.activation(w1_hl[:, 0, g, :], w1_sb[:, g, :], ACT.Copy).then_inc(w_hi_ready, 1)
                if q in W2_SPLIT:
                    nc.scalar.activation(w2_hl[:, 0], w2_sb[:], ACT.Copy).then_inc(w_hi_ready, 1)
                if q in Z_SPLIT:
                    g = Z_SPLIT[q]
                    if g == 0:
                        act.wait_ge(dense_in[0], 16 * DENSE)
                        act.wait_ge(u_ready, (BLOCKS - 1) * QUADS + z_quads)
                    done = (BLOCKS - 1) * BB
                    nc.scalar.activation(z_hl[:, 0, g, 0:done], zT[:, g, 0:done], ACT.Copy).then_inc(zs_hi_ready, 1)
                if q in Z_LAST_SPLIT:
                    z_last_round(Z_LAST_SPLIT[q])

            def z_last_round(g):
                h = g // 2
                act.wait_ge(dense_in[1 + h], 16 * sum(sg // 2 == h for sg, _ in SPARE_ROWS))
                done = (BLOCKS - 1) * BB
                nc.scalar.activation(z_hl[:, 0, g, done:], zT[:, g, done:], ACT.Copy).then_inc(zs_hi_ready, 1)

            for ch in range(KAHEAD):
                k_round(ch)
            for q in AHEAD:
                for _, t in SPLIT.get(q % QUADS, []):
                    split_tile(0, t)
                for _, t in SPREAD.get(q % QUADS, []):
                    spread_tile(0, t)

            def body(b, first, last):
                ch = KAHEAD
                for q in range(QUADS):
                    if q == ZLAG + 1 and not first:
                        z_evacuate(b - 1, 1)
                    if q == QUADS // 2 + ZLAG + 1:
                        if last:
                            z_evacuate_last(0)
                        else:
                            z_evacuate(b, 0)
                    for nxt, t in SPLIT.get(q, []):
                        if not (nxt and last):
                            split_tile(b + 1 if nxt else b, t)
                    for nxt, t in SPREAD.get(q, []):
                        if not (nxt and last):
                            spread_tile(b + 1 if nxt else b, t)
                    if first and q % 2 == 0 and ch < KCHUNKS:
                        k_round(ch)
                        ch += 1
                    if last:
                        mlp_round(q)

            over_blocks(act, body)
            z_evacuate_last(1)
            act.wait_ge(small_in, 48)

            def h1_out(n):
                m, cols = n % (HID1 // P), slice(n // (HID1 // P) * 512, (n // (HID1 // P) + 1) * 512)
                act.wait_ge(h1_ps_ready, n + 1)
                if n >= 4:
                    act.wait_ge(h1_ready, n - 3)
                nc.scalar.activation(h1_raw(n), h_ps(n), ACT.Relu, bias=b1_sb[:, m:m + 1]).then_inc(h1_relu, 1)
                act.wait_ge(h1_relu, n + 1)
                nc.scalar.activation(h1_hl[:, 0, m, cols], h1_raw(n), ACT.Copy).then_inc(h1_hi_ready, 1)

            h1_out(0)
            for g in (2, 3):
                z_last_round(g)
            for n in range(1, 8):
                h1_out(n)
            n = 8
            for hb in range(2):
                cols = slice(hb * 512, (hb + 1) * 512)
                for m in range(HID2 // P):
                    act.wait_ge(h2_ps_ready, n - 7)
                    nc.scalar.activation(h2T[:, m, cols], h_ps(n), ACT.Relu, bias=b2_sb[:, m:m + 1]).then_inc(h2_ready, 1)
                    n += 1
            for hb in range(2):
                act.wait_ge(y_ps_ready, hb + 1)
                nc.scalar.activation(y_sb[0:1, hb * 512:(hb + 1) * 512], h_ps(n)[0:1, :], ACT.Copy).then_inc(y_ready, 1)
                n += 1

        @block.vector
        def _(dve):
            nc.vector.memset(sel[:], 0.0).then_inc(sel_zero, 1)
            dve.wait_ge(sel_zero, 1)
            nc.vector.memset(sel[0:EMBED, 30:31], 1.0).then_inc(sel_ready, 1)
            nc.vector.memset(sel[EMBED:P, 31:32], 1.0).then_inc(sel_ready, 1)

            def k_rest(ch):
                dve.wait_ge(k_hi_ready, ch + 1)
                upper = k_split[EMBED:P, ch * KCOLS:(ch + 1) * KCOLS]
                nc.vector.tensor_tensor(upper, k_raw(ch % KST)[EMBED:P, :], upper, ALU.subtract).then_inc(k_ready, 1)

            def tile_rest(b, t):
                dve.wait_ge(rows_ready, b * TILES + t + 1)
                nc.vector.tensor_tensor(hl[:, t % HL, 1, :], rows[:, b % 2, t, :], hl[:, t % HL, 0, :],
                                        ALU.subtract).then_inc(lo_ready, 1)

            def mlp_rest(q):
                if q in W1_SPLIT:
                    g = W1_SPLIT[q]
                    dve.wait_ge(w_hi_ready, g + 1)
                    nc.vector.tensor_tensor(w1_hl[:, 1, g, :], w1_sb[:, g, :], w1_hl[:, 0, g, :], ALU.subtract).then_inc(w_ready, 1)
                if q in W2_SPLIT:
                    dve.wait_ge(w_hi_ready, ZGROUPS + 1)
                    nc.vector.tensor_tensor(w2_hl[:, 1], w2_sb[:], w2_hl[:, 0], ALU.subtract).then_inc(w_ready, 1)
                if q in Z_SPLIT:
                    g, done = Z_SPLIT[q], (BLOCKS - 1) * BB
                    dve.wait_ge(zs_hi_ready, g + 1)
                    nc.vector.tensor_tensor(z_hl[:, 1, g, 0:done], zT[:, g, 0:done], z_hl[:, 0, g, 0:done],
                                            ALU.subtract).then_inc(z_ready, 1)
                if q in Z_LAST_SPLIT:
                    z_last_rest(Z_LAST_SPLIT[q])

            def z_last_rest(g):
                done = (BLOCKS - 1) * BB
                dve.wait_ge(zs_hi_ready, ZGROUPS + g + 1)
                nc.vector.tensor_tensor(z_hl[:, 1, g, done:], zT[:, g, done:], z_hl[:, 0, g, done:],
                                        ALU.subtract).then_inc(z_ready, 1)

            for ch in range(KAHEAD):
                k_rest(ch)
            for q in AHEAD:
                for _, t in REST.get(q % QUADS, []):
                    tile_rest(0, t)

            def body(b, first, last):
                ch = KAHEAD
                for q in range(QUADS):
                    for nxt, t in REST.get(q, []):
                        if not (nxt and last):
                            tile_rest(b + 1 if nxt else b, t)
                    if first and q % 2 == 0 and ch < KCHUNKS:
                        k_rest(ch)
                        ch += 1
                    if last:
                        mlp_rest(q)
                    dve.wait_ge(u_ready, b * QUADS + q + 1)
                    if not first or q >= PROD:
                        dve.wait_ge(summed, b * QUADS + q - PROD + 1)
                    for k, count, t in runs(q):
                        op = nc.vector.tensor_tensor(prod[:, q % PROD, k:k + count, :], u_ps[q % 2][:, k:k + count, :],
                                                     rows[:, b % 2, t:t + count, :], ALU.mult)
                    op.then_inc(prod_ready, 1)

            over_blocks(dve, body)

            def h1_rest(n):
                m, cols = n % (HID1 // P), slice(n // (HID1 // P) * 512, (n // (HID1 // P) + 1) * 512)
                dve.wait_ge(h1_hi_ready, n + 1)
                nc.vector.tensor_tensor(h1_hl[:, 1, m, cols], h1_raw(n), h1_hl[:, 0, m, cols], ALU.subtract).then_inc(h1_ready, 1)

            h1_rest(0)
            for g in (2, 3):
                z_last_rest(g)
            for n in range(1, 8):
                h1_rest(n)

        @block.tensor
        def _(pe):
            def transpose(b, t):
                pe.wait_ge(gathered[t % NAT], 64 * (b * (TILES // NAT) + t // NAT + 1))
                if not (isinstance(b, int) and b == 0 and t == 0):
                    pe.wait_ge(rows_ready, b * TILES + t)
                for s in range(SUB):
                    op = nc.tensor.transpose(t_ps[:, s * P:(s + 1) * P], nat[:, t % NAT, s, :], ident[:])
                op.then_inc(transposed, 1)

            def interact(b, q, first):
                if not first or q >= 2:
                    pe.wait_ge(prod_ready, b * QUADS + q - 1)
                if first and q % (KCHUNK // QUAD) == 0:
                    ch = q // (KCHUNK // QUAD)
                    pe.wait_ge(k_ready, ch + 1)
                for k in range(QUAD):
                    n = QUAD * q + k
                    c, t = UNITS[n]
                    ct = c // 2
                    if t == 0:
                        pe.wait_ge(mov_ready, b * TILES + ct + 1)
                    for part in range(2):
                        op = nc.tensor.matmul(u_ps[q % 2][:, k, :], k_split[:, n * P:(n + 1) * P],
                                              mov[:, ct % MOV, c % 2, part, :], start=part == 0, stop=part == 1)
                op.then_inc(u_ready, 1)

            def add_up(b, q):
                group, slot = divmod(q, SLOTS)
                pe.wait_ge(prod_ready, b * QUADS + q + 1)
                if q % (QUADS // 2) == 0 and not (isinstance(b, int) and b == 0):
                    pe.wait_ge(z_out, 2 * (b - 1) + q // (QUADS // 2) + 1)
                for k in range(QUAD):
                    op = nc.tensor.matmul(z_ps[group // 2][32 * k:32 * k + 32, group % 2, :],
                                          sel[:, 30 - 2 * slot:62 - 2 * slot], prod[:, q % PROD, k, :],
                                          start=slot == 0, stop=slot == SLOTS - 1)
                op.then_inc(summed, 1)

            pe.wait_ge(ident_ready, 1)
            pe.wait_ge(sel_ready, 2)
            for q in AHEAD:
                for _, t in SPLIT.get(q % QUADS, []):
                    transpose(0, t)

            def body(b, first, last):
                for q in range(QUADS):
                    for nxt, t in SPLIT.get(q, []):
                        if not (nxt and last):
                            transpose(b + 1 if nxt else b, t)
                    interact(b, q, first)
                    if q >= ZLAG:
                        add_up(b, q - ZLAG)
                    elif not first:
                        add_up(b - 1, q - ZLAG + QUADS)

            over_blocks(pe, body)
            for q in range(QUADS - ZLAG, QUADS):
                add_up(BLOCKS - 1, q)

            def split_product(acc, weights, moving, parts, m, cols):
                for g in range(parts):
                    for x, y in ((0, 0), (1, 0), (0, 1)):
                        op = nc.tensor.matmul(acc, weights[:, x, g, m * P:(m + 1) * P], moving[:, y, g, cols],
                                              start=(g, x, y) == (0, 0, 0), stop=(g, x, y) == (parts - 1, 0, 1))
                return op

            pe.wait_ge(w_ready, ZGROUPS + 1)
            n = 0
            for hb in range(2):
                pe.wait_ge(z_ready, (1 + hb) * ZGROUPS)
                if hb == 0:
                    pe.wait_ge(prod_ready, BLOCKS * QUADS)
                for m in range(HID1 // P):
                    if n >= 4:
                        pe.wait_ge(h1_relu, n - 3)
                    split_product(h_ps(n), w1_hl, z_hl, ZGROUPS, m, slice(hb * 512, (hb + 1) * 512)).then_inc(h1_ps_ready, 1)
                    n += 1
            for hb in range(2):
                pe.wait_ge(h1_ready, 4 * (hb + 1))
                for m in range(HID2 // P):
                    if n < 12:
                        pe.wait_ge(h1_relu, min(8, n - 3))
                    split_product(h_ps(n), w2_hl, h1_hl, HID1 // P, m, slice(hb * 512, (hb + 1) * 512)).then_inc(h2_ps_ready, 1)
                    n += 1
            for hb in range(2):
                cols = slice(hb * 512, (hb + 1) * 512)
                pe.wait_ge(h2_ready, 2 * (hb + 1))
                for g in range(HID2 // P):
                    op = nc.tensor.matmul(h_ps(n)[0:1, :], w3_sb[:, g:g + 1], h2T[:, g, cols],
                                          start=g == 0, stop=g == HID2 // P - 1)
                op.then_inc(y_ps_ready, 1)
                n += 1


def kernel(**inputs):
    import concourse.bacc as bacc
    from concourse.bass_utils import run_bass_kernel_spmd

    nc = bacc.Bacc("TRN2", target_bir_lowering=False, num_devices=1)
    arrays = {}

    def dram(name, a):
        a = np.ascontiguousarray(a)
        arrays[name] = a
        return nc.dram_tensor(name, a.shape, mybir.dt.from_np(a.dtype), kind="ExternalInput").ap()

    k_in = np.asarray(inputs["L0_rec_kernel"])
    w1_in = np.asarray(inputs["W_top1"])
    first = [r * (2 * FIELDS - r - 1) // 2 - r - 1 for r in range(FIELDS)]
    k_units = np.zeros((EMBED, len(UNITS), 2, EMBED), k_in.dtype)
    w1_rows = np.zeros((ZGROUPS, P, HID1), w1_in.dtype)
    spare = 0
    for n, (c, t) in enumerate(UNITS):
        for h in range(2):
            r = 2 * t + h
            if r < c:
                k_units[:, n, h] = k_in[:, first[r] + c]
                w1_rows[z_row(n, h)] = w1_in[first[r] + c]
            else:
                w1_rows[z_row(n, h)] = w1_in[PAIRS + spare]
                spare += 1
    kern = k_units.reshape(EMBED, KCHUNKS, KCOLS).transpose(1, 0, 2)
    ids = np.asarray(inputs["ids"]).reshape(BATCH // P, P, FIELDS).transpose(1, 0, 2).reshape(P, -1).view(np.uint32)

    args = [dram("ids", ids), [dram(f"tbl_{f}", np.asarray(inputs[f"tbl_{f}"])) for f in range(FIELDS)],
            dram("kern", kern), dram("dense", np.asarray(inputs["dense_ctx"]).T),
            dram("w1", w1_rows.transpose(1, 0, 2)), dram("b1", np.asarray(inputs["b_top1"]).reshape(-1, P).T),
            dram("w2", np.asarray(inputs["W_top2"]).reshape(-1, P, HID2).transpose(1, 0, 2)),
            dram("b2", np.asarray(inputs["b_top2"]).reshape(-1, P).T),
            dram("w3", np.asarray(inputs["W_top3"]).reshape(-1, P).T)]
    out = nc.dram_tensor("out", (1, BATCH), mybir.dt.float32, kind="ExternalOutput").ap()
    tower(nc, *args, out)
    r = run_bass_kernel_spmd(nc, [arrays], core_ids=[0])
    return r.results[0]["out"].reshape(BATCH, 1)
```

```python
import numpy as np
import concourse.bass as bass
from concourse import mybir
from contextlib import ExitStack

BATCH, FIELDS, EMBED, DENSE = 1024, 32, 64, 16
PAIRS = FIELDS * (FIELDS - 1) // 2
HID1, HID2 = 512, 256
P = 128

BB = 256
BLOCKS = BATCH // BB
SUB = BB // P
TILES = FIELDS // 2
UNITS = [(c, t) for c in range(1, FIELDS) for t in range((c + 1) // 2)]
QUAD = 4
QUADS = len(UNITS) // QUAD
ZGROUPS = 4
SLOTS = QUADS // ZGROUPS
assert len(UNITS) == 256 and SLOTS * 2 == 32

KCHUNK = 16
KCHUNKS = len(UNITS) // KCHUNK
KHALF = KCHUNK // 2 * P
KQUADS = KCHUNK // QUAD

NAT, HL, MOV, PROD, KST, KLOADS = 4, 4, 4, 4, 3, 3
ZLAG = 2
ZOUT_AT = 14


def z_row(n, h):
    q, tile = divmod(n, QUAD)
    pair, second = divmod(q, 2)
    return 2 * (pair // SLOTS) + second, 32 * tile + 2 * (pair % SLOTS) + h


def last_quad(t):
    return ((t + 1) ** 2 - 1) // QUAD


def first_quad(t):
    return t * t // QUAD if t else -1


SPLIT_AT = [-12, -10, -8, -4, -2, 0, 4, 6] + [(first_quad(t) - 5) // 2 * 2 for t in range(8, TILES)]
REST_AT = [q + 2 for q in SPLIT_AT]
SPREAD_AT = [max(SPLIT_AT[t] + 3, last_quad((t - MOV) % TILES) - (QUADS if t < MOV else 0) + 1) for t in range(TILES)]
SPREAD_AT[4:7] = [2, 4, 6]

LEAD0 = [1, 1, 1, 1, 2, 2, 3, 4, 5, 6, 7, 7, 7, 7, 7, 7]
SPLIT0_AT = [first_quad(t) - LEAD0[t] for t in range(TILES)]
REST0_AT = [q + (LEAD0[t] > 3) for t, q in enumerate(SPLIT0_AT)]
SPREAD0_AT = [max(SPLIT0_AT[t] + (2 if LEAD0[t] > 3 else 0), last_quad(t - MOV) + 1 if t >= MOV else -2) for t in range(TILES)]
for split, spread in ((SPLIT_AT, SPREAD_AT), (SPLIT0_AT, SPREAD0_AT)):
    assert all(spread[t] <= first_quad(t) for t in range(TILES)) and spread == sorted(spread)
    assert all(spread[t - HL] < split[t] for t in range(HL, TILES))
assert all(SPREAD_AT[t - HL] - QUADS < SPLIT_AT[t] and SPREAD0_AT[t - HL] - QUADS < SPLIT_AT[t] for t in range(HL))

K_AT = [-3, -2, 0, 2, 4, 7, 9, 12, 15, 19, 23, 27, 31, 36, 41, 46]
KPIECES = 2
K_REST_AT = [[K_AT[ch] + (K_AT[ch] >= 0) * (1 + p * (K_AT[min(ch + 1, KCHUNKS - 1)] - K_AT[ch]) // KPIECES)
              for p in range(KPIECES)] for ch in range(KCHUNKS)]
assert all(at[-1] < KQUADS * ch for ch, at in enumerate(K_REST_AT))
K_POOL = (10, 12, 14, 15)


def k_lo_count(ch):
    return sum((n in K_POOL) == (ch in K_POOL) for n in range(ch + 1))


def events(at, at0):
    def due(q, first):
        own = [(False, t) for t, x in enumerate(at0 if first else at) if x == q]
        return own + [(True, t) for t, x in enumerate(at) if x < 0 and x + QUADS == q]
    return due


SPLIT, REST, SPREAD = events(SPLIT_AT, SPLIT0_AT), events(REST_AT, REST0_AT), events(SPREAD_AT, SPREAD0_AT)
AHEAD = range(min(SPLIT0_AT + K_AT), 0)


SPARE_ROWS = [z_row(n, 1) for n, (c, t) in enumerate(UNITS) if c == 2 * t + 1]
assert len(SPARE_ROWS) == DENSE

W1_SPLIT = {28: 0, 31: 1, 34: 2, 37: 3}
W2_SPLIT = {40: 0}
Z_SPLIT = {45: 0, 48: 1, 51: 2, 54: 3}
Z_LAST_SPLIT = {58: 0, 60: 1}


def runs(q):
    out = []
    for k in range(QUAD):
        c, t = UNITS[QUAD * q + k]
        if out and UNITS[QUAD * q + k - 1][0] == c:
            out[-1][1] += 1
        else:
            out.append([k, 1, t])
    return out


def tower(nc, ids, tables, kern, dense, w1, b1, w2, b2, w3, out):
    f32, f32r, u32 = mybir.dt.float32, mybir.dt.float32r, mybir.dt.uint32
    ALU, ACT = mybir.AluOpType, mybir.ActivationFunctionType
    with ExitStack() as ctx:
        def sb(name, shape, dt=f32):
            return ctx.enter_context(nc.sbuf_tensor(name, shape, dt))

        def pb(name, shape):
            return ctx.enter_context(nc.psum_tensor(name, shape, f32))

        def sem(name):
            return ctx.enter_context(nc.semaphore(name))

        z_dram = nc.dram_tensor("z_dram", (ZGROUPS, P, BATCH), f32, kind="Internal").ap()

        with nc.sbuf_tensor("k_split", [P, len(UNITS) * P], f32r) as k_split:
            pass
        with nc.sbuf_tensor("k_first_half", [P, KCHUNKS * KHALF], f32), \
                nc.sbuf_tensor("k_raw_sb", [P, KCHUNKS, KHALF], f32) as k_raw_sb:
            pass
        over, over_bytes = ExitStack(), [0]
        with over:
            def sb2(name, shape, dt=f32):
                over_bytes[0] += 4 * int(np.prod(shape[1:]))
                return (over.enter_context(nc.sbuf_tensor(name, shape, dt)),
                        min(QUADS, -(-over_bytes[0] // (4 * P * QUAD))))
            w1_sb, _ = sb2("w1_sb", [P, ZGROUPS, HID1])
            w2_sb, _ = sb2("w2_sb", [P, HID1 // P, HID2])
            zT, mlp_raw_quads = sb2("zT", [P, ZGROUPS, BATCH])
            w1_hl, _ = sb2("w1_hl", [P, 2, ZGROUPS, HID1], f32r)
            w2_hl, w_quads = sb2("w2_hl", [P, 2, HID1 // P, HID2], f32r)
            z_hl, z_quads = sb2("z_hl", [P, 2, ZGROUPS, BATCH], f32r)
            h1_hl, _ = sb2("h1_hl", [P, 2, HID1 // P, BATCH], f32r)
            h2T, _ = sb2("h2T", [P, HID2 // P, BATCH])
            y_sb, _ = sb2("y_sb", [P, BATCH // QUAD])
        assert over_bytes[0] <= 4 * P * len(UNITS)
        ctx.enter_context(nc.sbuf_tensor("k_split_space", [P, len(UNITS) * P], f32r))

        rows = sb("rows", [P, 2, TILES, BB])
        nat = sb("nat", [P, NAT, SUB, P])
        hl = sb("hl", [P, HL, 2, BB], f32r)
        mov = sb("mov", [P, MOV, 2, 2, BB], f32r)
        prod = sb("prod", [P, PROD, QUAD, BB])
        z_sb = sb("z_sb", [P, 2, BB])
        ids_sb = sb("ids_sb", [P, BATCH // P * FIELDS], u32)
        ident = sb("ident", [P, P])
        sel = sb("sel", [P, 62])
        w3_sb = sb("w3_sb", [P, HID2 // P])
        b1_sb = sb("b1_sb", [P, HID1 // P])
        b2_sb = sb("b2_sb", [P, HID2 // P])

        def k_raw(ch):
            if ch < KCHUNKS - 1:
                return k_raw_sb[:, ch, :]
            return rows[:, 1, 4 * KST:4 * KST + 4, :].rearrange("p a b -> p (a b)")

        def k_hi(ch):
            s = ch % KST
            return rows[:, 1, 4 * s:4 * s + 4, :].rearrange("p a b -> p (a b)").bitcast(f32r)

        def h1_raw(n):
            return w1_sb[:, n % 4, :]

        u_ps = [pb(f"u_ps{s}", [P, QUAD, BB]) for s in range(2)]
        t_ps = pb("t_ps", [P, BB])
        z_ps = [pb(f"z_ps{h}", [P, 2, BB]) for h in range(2)]

        ids_in, ident_zero, ident_ready = sem("ids_in"), sem("ident_zero"), sem("ident_ready")
        sel_zero, sel_ready = sem("sel_zero"), sem("sel_ready")
        gathered = [sem(f"gathered{s}") for s in range(NAT)]
        transposed, rows_ready, lo_ready, mov_ready = sem("transposed"), sem("rows_ready"), sem("lo_ready"), sem("mov_ready")
        k_in = [sem(f"k_in{s}") for s in range(KLOADS)]
        k_hi_ready, k_lo_ready, k_lo_pool = sem("k_hi_ready"), sem("k_lo_ready"), sem("k_lo_pool")
        k_ready = [sem(f"k_ready{s}") for s in range(KST)]
        u_ready, prod_ready, summed = sem("u_ready"), sem("prod_ready"), sem("summed")
        z_out = sem("z_out")
        z_saved = sem("z_saved")
        small_in, w_in, z_back = sem("small_in"), sem("w_in"), sem("z_back")
        z_last_out, z_last_ready = sem("z_last_out"), sem("z_last_ready")
        dense_in = [sem(f"dense_in{n}") for n in range(3)]
        w_hi_ready, w_ready, zs_hi_ready, z_ready = sem("w_hi_ready"), sem("w_ready"), sem("zs_hi_ready"), sem("z_ready")
        h1_ps_ready, h1_relu, h1_hi_ready, h1_ready = sem("h1_ps_ready"), sem("h1_relu"), sem("h1_hi_ready"), sem("h1_ready")
        h2_ps_ready, h2_ready = sem("h2_ps_ready"), sem("h2_ready")
        y_ps_ready, y_ready, stored = sem("y_ps_ready"), sem("y_ready"), sem("stored")

        def over_blocks(eng, body):
            body(0, True, False)
            with eng.Fori(1, BLOCKS - 1) as b:
                body(b, False, False)
            body(BLOCKS - 1, False, True)

        def h_ps(n):
            return u_ps[(n // 2) % 2][:, 2 * (n % 2):2 * (n % 2) + 2, :].rearrange("p a b -> p (a b)")

        def y_ps(k):
            return h_ps(12 + k % 2)[32 * k:32 * k + 1, 0:BB]

        block = ctx.enter_context(nc.Block())

        @block.gpsimd
        def _(pool):
            nc.gpsimd.memset(ident[:], 0.0).then_inc(ident_zero, 1)
            pool.wait_ge(ident_zero, 1)
            nc.gpsimd.affine_select(out=ident[:], in_=ident[:], compare_op=ALU.not_equal, fill=1.0, base=0,
                                    pattern=[[-1, P]], channel_multiplier=1).then_inc(ident_ready, 1)
            pool.wait_ge(ids_in, 16)
            def look_up(T):
                b, t = divmod(T, TILES)
                if T >= NAT:
                    pool.wait_ge(transposed, T - NAT + 1)
                for f in (2 * t, 2 * t + 1):
                    for s in range(SUB):
                        col = (SUB * b + s) * FIELDS + f
                        pool.indirect_dma_start(
                            nat[:, T % NAT, s, (f % 2) * EMBED:(f % 2 + 1) * EMBED], None, tables[f],
                            bass.IndirectOffsetOnAxis(ids_sb[:, col:col + 1], 0)).then_inc(gathered[T % NAT], 16)

            def k_rest(ch, T):
                for s in range(NAT):
                    pool.wait_ge(gathered[s], 64 * len(range(s, T, NAT)))
                pool.wait_ge(k_hi_ready, ch + 1)
                nc.gpsimd.tensor_tensor(k_raw(ch).bitcast(f32r), k_raw(ch), k_hi(ch), ALU.subtract).then_inc(k_lo_pool, 1)

            chunks = list(K_POOL)
            for T in range(BLOCKS * TILES):
                freed = T - NAT
                quad = -QUADS if freed < 0 else SPLIT0_AT[freed] if freed < TILES else QUADS * (freed // TILES) + SPLIT_AT[freed % TILES]
                while chunks and K_AT[chunks[0]] <= quad:
                    k_rest(chunks.pop(0), T)
                look_up(T)

            for s in range(NAT):
                pool.wait_ge(gathered[s], 64 * BLOCKS * TILES // NAT)
            done = (BLOCKS - 1) * BB
            for g in range(ZGROUPS):
                pool.wait_ge(w_hi_ready, g + 1)
                nc.gpsimd.tensor_tensor(w1_hl[:, 1, g, :], w1_sb[:, g, :], w1_hl[:, 0, g, :], ALU.subtract).then_inc(w_ready, 1)
            pool.wait_ge(w_hi_ready, ZGROUPS + 1)
            nc.gpsimd.tensor_tensor(w2_hl[:, 1], w2_sb[:], w2_hl[:, 0], ALU.subtract).then_inc(w_ready, 1)
            for g in range(ZGROUPS):
                pool.wait_ge(zs_hi_ready, g + 1)
                nc.gpsimd.tensor_tensor(z_hl[:, 1, g, 0:done], zT[:, g, 0:done], z_hl[:, 0, g, 0:done],
                                        ALU.subtract).then_inc(z_ready, 1)
            for g in range(2):
                pool.wait_ge(zs_hi_ready, ZGROUPS + g + 1)
                nc.gpsimd.tensor_tensor(z_hl[:, 1, g, done:], zT[:, g, done:], z_hl[:, 0, g, done:],
                                        ALU.subtract).then_inc(z_ready, 1)

        @block.sync
        def _(sp):
            sp.dma_start(ids_sb[:], ids).then_inc(ids_in, 16)
            def k_load(ch):
                sp.dma_start(k_raw(ch), kern[ch]).then_inc(k_in[ch % KLOADS], 16)

            for ch in range(KLOADS):
                k_load(ch)
            for ch in range(KCHUNKS):
                s, col = ch % KST, ch * KCHUNK * P
                sp.wait_ge(k_lo_pool if ch in K_POOL else k_lo_ready, k_lo_count(ch))
                under = min(2 * ch - KCHUNKS + 1, KCHUNKS - 2)
                if under >= 0:
                    sp.wait_ge(k_ready[under % KST], 64 * (under // KST + 1))
                for half in range(2):
                    cols = slice(col + half * KHALF, col + (half + 1) * KHALF)
                    src = slice(EMBED * half, EMBED * (half + 1))
                    sp.dma_start(k_split[0:EMBED, cols].bitcast(f32), k_hi(ch)[src, :].bitcast(f32)).then_inc(k_ready[s], 16)
                    sp.dma_start(k_split[EMBED:P, cols].bitcast(f32), k_raw(ch)[src, :]).then_inc(k_ready[s], 16)
                if ch + KLOADS < KCHUNKS:
                    k_load(ch + KLOADS)
            sp.dma_start(w3_sb[:], w3).then_inc(small_in, 16)
            sp.dma_start(b1_sb[:], b1).then_inc(small_in, 16)
            sp.dma_start(b2_sb[:], b2).then_inc(small_in, 16)

            done = (BLOCKS - 1) * BB
            sp.wait_ge(u_ready, (BLOCKS - 1) * QUADS + mlp_raw_quads)
            sp.dma_start(w1_sb[:], w1).then_inc(w_in, 16)
            sp.dma_start(w2_sb[:], w2).then_inc(w_in, 16)
            sp.wait_ge(z_saved, 32 * (BLOCKS - 1))
            sp.dma_start(zT[:, :, 0:done], z_dram[:, :, 0:done].rearrange("g p n -> p g n")).then_inc(z_back, 16)

            def dense_rows(groups, cols, landed):
                for k, (g, r) in enumerate(SPARE_ROWS):
                    if g in groups:
                        sp.dma_start(zT[r:r + 1, g, cols], dense[k:k + 1, cols]).then_inc(landed, 16)

            sp.wait_ge(z_back, 16)
            dense_rows((0, 1, 2, 3), slice(0, done), dense_in[0])
            for h in range(2):
                sp.wait_ge(z_last_out, h + 1)
                dense_rows((2 * h, 2 * h + 1), slice(done, BATCH), dense_in[1 + h])
            sp.wait_ge(y_ready, 4)
            sp.dma_start(out.rearrange("o (k n) -> (o k) n", k=QUAD), y_sb[0:P:32, :]).then_inc(stored, 16)
            sp.wait_ge(stored, 16)

        @block.scalar
        def _(act):
            def k_round(ch):
                act.wait_ge(k_in[ch % KLOADS], 16 * (ch // KLOADS + 1))
                if ch >= KST:
                    act.wait_ge(k_ready[ch % KST], 64 * (ch // KST))
                nc.scalar.activation(k_hi(ch), k_raw(ch), ACT.Copy).then_inc(k_hi_ready, 1)

            def split_tile(b, t):
                first, second = isinstance(b, int) and b == 0, isinstance(b, int) and b == 1
                act.wait_ge(transposed, b * TILES + t + 1)
                nc.scalar.activation(hl[:, t % HL, 0, :], t_ps[:], ACT.Copy)
                if t == 0 and second:
                    for s in range(KST):
                        act.wait_ge(k_ready[s], 64 * len(range(s, KCHUNKS, KST)))
                elif t == 0 and not first:
                    act.wait_ge(prod_ready, (b - 1) * QUADS)
                nc.scalar.activation(rows[:, b % 2, t, :], t_ps[:], ACT.Copy).then_inc(rows_ready, 1)

            def spread_tile(b, t):
                act.wait_ge(lo_ready, b * TILES + t + 1)
                if t >= MOV:
                    act.wait_ge(u_ready, b * QUADS + last_quad(t - MOV) + 1)
                elif not (isinstance(b, int) and b == 0):
                    act.wait_ge(u_ready, (b - 1) * QUADS + last_quad(t - MOV + TILES) + 1)
                for f in range(2):
                    for half in range(2):
                        op = nc.scalar.activation(mov[EMBED * half:EMBED * (half + 1), t % MOV, f],
                                                  hl[EMBED * f:EMBED * (f + 1), t % HL], ACT.Copy)
                op.then_inc(mov_ready, 1)

            def z_evacuate(b, h):
                act.wait_ge(summed, b * QUADS + (h + 1) * (QUADS // 2))
                if not (isinstance(b, int) and b == 0 and h == 0):
                    act.wait_ge(z_saved, 32 * b + 16 * h)
                nc.scalar.activation(z_sb[:], z_ps[h][:], ACT.Copy).then_inc(z_out, 1)
                act.wait_ge(z_out, 2 * b + h + 1)
                act.dma_start(z_dram[2 * h:2 * h + 2, :, bass.ds(b * BB, BB)].rearrange("g p n -> p g n"),
                              z_sb[:]).then_inc(z_saved, 16)

            def z_evacuate_last(h):
                act.wait_ge(summed, (BLOCKS - 1) * QUADS + (h + 1) * (QUADS // 2))
                nc.scalar.activation(zT[:, 2 * h:2 * h + 2, (BLOCKS - 1) * BB:], z_ps[h][:], ACT.Copy).then_inc(z_last_out, 1)

            def mlp_round(q):
                if q in W1_SPLIT:
                    g = W1_SPLIT[q]
                    if g == 0:
                        act.wait_ge(w_in, 32)
                        act.wait_ge(u_ready, (BLOCKS - 1) * QUADS + w_quads)
                    nc.scalar.activation(w1_hl[:, 0, g, :], w1_sb[:, g, :], ACT.Copy).then_inc(w_hi_ready, 1)
                if q in W2_SPLIT:
                    nc.scalar.activation(w2_hl[:, 0], w2_sb[:], ACT.Copy).then_inc(w_hi_ready, 1)
                if q in Z_SPLIT:
                    g = Z_SPLIT[q]
                    if g == 0:
                        act.wait_ge(dense_in[0], 16 * DENSE)
                        act.wait_ge(u_ready, (BLOCKS - 1) * QUADS + z_quads)
                    done = (BLOCKS - 1) * BB
                    nc.scalar.activation(z_hl[:, 0, g, 0:done], zT[:, g, 0:done], ACT.Copy).then_inc(zs_hi_ready, 1)
                if q in Z_LAST_SPLIT:
                    z_last_round(Z_LAST_SPLIT[q])

            def z_last_round(g):
                h = g // 2
                act.wait_ge(dense_in[1 + h], 16 * sum(sg // 2 == h for sg, _ in SPARE_ROWS))
                done = (BLOCKS - 1) * BB
                nc.scalar.activation(z_hl[:, 0, g, done:], zT[:, g, done:], ACT.Copy).then_inc(zs_hi_ready, 1)

            for q in AHEAD:
                for _, t in SPLIT(q, True):
                    split_tile(0, t)
                for _, t in SPREAD(q, True):
                    spread_tile(0, t)
                for ch in range(KCHUNKS):
                    if K_AT[ch] == q:
                        k_round(ch)

            def body(b, first, last):
                for q in range(QUADS):
                    if q == ZOUT_AT and not first:
                        z_evacuate(b - 1, 1)
                    if q == QUADS // 2 + (ZLAG + 1 if last else ZOUT_AT):
                        if last:
                            z_evacuate_last(0)
                        else:
                            z_evacuate(b, 0)
                    for nxt, t in SPLIT(q, first):
                        if not (nxt and last):
                            split_tile(b + 1 if nxt else b, t)
                    for nxt, t in SPREAD(q, first):
                        if not (nxt and last):
                            spread_tile(b + 1 if nxt else b, t)
                    for ch in range(KCHUNKS):
                        if first and K_AT[ch] == q:
                            k_round(ch)
                    if last:
                        mlp_round(q)

            over_blocks(act, body)
            z_evacuate_last(1)
            act.wait_ge(small_in, 48)

            def h1_out(n):
                m, cols = n % (HID1 // P), slice(n // (HID1 // P) * 512, (n // (HID1 // P) + 1) * 512)
                act.wait_ge(h1_ps_ready, n + 1)
                if n >= 4:
                    act.wait_ge(h1_ready, n - 3)
                nc.scalar.activation(h1_raw(n), h_ps(n), ACT.Relu, bias=b1_sb[:, m:m + 1]).then_inc(h1_relu, 1)
                act.wait_ge(h1_relu, n + 1)
                nc.scalar.activation(h1_hl[:, 0, m, cols], h1_raw(n), ACT.Copy).then_inc(h1_hi_ready, 1)

            h1_out(0)
            for g in (2, 3):
                z_last_round(g)
            for n in range(1, 8):
                h1_out(n)
            n = 8
            for hb in range(2):
                cols = slice(hb * 512, (hb + 1) * 512)
                for m in range(HID2 // P):
                    act.wait_ge(h2_ps_ready, n - 7)
                    nc.scalar.activation(h2T[:, m, cols], h_ps(n), ACT.Relu, bias=b2_sb[:, m:m + 1]).then_inc(h2_ready, 1)
                    n += 1
            act.wait_ge(y_ps_ready, 1)
            for k in (0, 2):
                nc.scalar.activation(y_sb[32 * k:32 * k + 1, :], y_ps(k), ACT.Copy).then_inc(y_ready, 1)

        @block.vector
        def _(dve):
            nc.vector.memset(sel[:], 0.0).then_inc(sel_zero, 1)
            dve.wait_ge(sel_zero, 1)
            nc.vector.memset(sel[0:EMBED, 30:31], 1.0).then_inc(sel_ready, 1)
            nc.vector.memset(sel[EMBED:P, 31:32], 1.0).then_inc(sel_ready, 1)

            def k_rest(ch, q):
                size = KHALF // KPIECES
                for p in range(0 if ch in K_POOL else KPIECES):
                    if K_REST_AT[ch][p] == q:
                        piece = slice(p * size, (p + 1) * size)
                        if p == 0:
                            dve.wait_ge(k_hi_ready, ch + 1)
                        op = nc.vector.tensor_tensor(k_raw(ch)[:, piece].bitcast(f32r), k_raw(ch)[:, piece], k_hi(ch)[:, piece],
                                                     ALU.subtract)
                        if p == KPIECES - 1:
                            op.then_inc(k_lo_ready, 1)

            def tile_rest(b, t):
                dve.wait_ge(rows_ready, b * TILES + t + 1)
                nc.vector.tensor_tensor(hl[:, t % HL, 1, :], rows[:, b % 2, t, :], hl[:, t % HL, 0, :],
                                        ALU.subtract).then_inc(lo_ready, 1)

            def z_last_rest(g):
                done = (BLOCKS - 1) * BB
                dve.wait_ge(zs_hi_ready, ZGROUPS + g + 1)
                nc.vector.tensor_tensor(z_hl[:, 1, g, done:], zT[:, g, done:], z_hl[:, 0, g, done:],
                                        ALU.subtract).then_inc(z_last_ready, 1)

            for q in AHEAD:
                for _, t in REST(q, True):
                    tile_rest(0, t)
                for ch in range(KCHUNKS):
                    k_rest(ch, q)

            def body(b, first, last):
                for q in range(QUADS):
                    for nxt, t in REST(q, first):
                        if not (nxt and last):
                            tile_rest(b + 1 if nxt else b, t)
                    for ch in range(KCHUNKS if first else 0):
                        k_rest(ch, q)
                    dve.wait_ge(u_ready, b * QUADS + q + 1)
                    if not first or q >= PROD:
                        dve.wait_ge(summed, b * QUADS + q - PROD + 1)
                    for k, count, t in runs(q):
                        op = nc.vector.tensor_tensor(prod[:, q % PROD, k:k + count, :], u_ps[q % 2][:, k:k + count, :],
                                                     rows[:, b % 2, t:t + count, :], ALU.mult)
                    op.then_inc(prod_ready, 1)

            over_blocks(dve, body)

            def h1_rest(n):
                m, cols = n % (HID1 // P), slice(n // (HID1 // P) * 512, (n // (HID1 // P) + 1) * 512)
                dve.wait_ge(h1_hi_ready, n + 1)
                nc.vector.tensor_tensor(h1_hl[:, 1, m, cols], h1_raw(n), h1_hl[:, 0, m, cols], ALU.subtract).then_inc(h1_ready, 1)

            h1_rest(0)
            for g in (2, 3):
                z_last_rest(g)
            for n in range(1, 8):
                h1_rest(n)
            dve.wait_ge(y_ps_ready, 1)
            for k in (1, 3):
                nc.vector.tensor_copy(y_sb[32 * k:32 * k + 1, :], y_ps(k)).then_inc(y_ready, 1)

        @block.tensor
        def _(pe):
            def transpose(b, t):
                pe.wait_ge(gathered[t % NAT], 64 * (b * (TILES // NAT) + t // NAT + 1))
                if not (isinstance(b, int) and b == 0 and t == 0):
                    pe.wait_ge(rows_ready, b * TILES + t)
                for s in range(SUB):
                    op = nc.tensor.transpose(t_ps[:, s * P:(s + 1) * P], nat[:, t % NAT, s, :], ident[:])
                op.then_inc(transposed, 1)

            def interact(b, q, first):
                if not first or q >= 2:
                    pe.wait_ge(prod_ready, b * QUADS + q - 1)
                if first and q % KQUADS == 0:
                    ch = q // KQUADS
                    pe.wait_ge(k_ready[ch % KST], 64 * (ch // KST + 1))
                for k in range(QUAD):
                    n = QUAD * q + k
                    c, t = UNITS[n]
                    ct = c // 2
                    if t == 0:
                        pe.wait_ge(mov_ready, b * TILES + ct + 1)
                    for part in range(2):
                        op = nc.tensor.matmul(u_ps[q % 2][:, k, :], k_split[:, n * P:(n + 1) * P],
                                              mov[:, ct % MOV, c % 2, part, :], start=part == 0, stop=part == 1)
                op.then_inc(u_ready, 1)

            def add_up(b, q):
                half, slot = divmod(q // 2, SLOTS)
                pe.wait_ge(prod_ready, b * QUADS + q + 2)
                if slot == 0 and not (isinstance(b, int) and b == 0):
                    pe.wait_ge(z_out, 2 * (b - 1) + half + 1)
                for k in range(QUAD):
                    op = nc.tensor.matmul(z_ps[half][32 * k:32 * k + 32, :, :], sel[:, 30 - 2 * slot:62 - 2 * slot],
                                          prod[:, q % PROD:q % PROD + 2, k, :], start=slot == 0, stop=slot == SLOTS - 1)
                op.then_inc(summed, 2)

            pe.wait_ge(ident_ready, 1)
            pe.wait_ge(sel_ready, 2)
            for q in AHEAD:
                for _, t in SPLIT(q, True):
                    transpose(0, t)

            def body(b, first, last):
                for q in range(QUADS):
                    for nxt, t in SPLIT(q, first):
                        if not (nxt and last):
                            transpose(b + 1 if nxt else b, t)
                    interact(b, q, first)
                    if q % 2:
                        if q > ZLAG:
                            add_up(b, q - ZLAG - 1)
                        elif not first:
                            add_up(b - 1, q - ZLAG - 1 + QUADS)

            over_blocks(pe, body)

            def split_product(acc, weights, moving, parts, m, cols):
                for g in range(parts):
                    for x, y in ((0, 0), (1, 0), (0, 1)):
                        op = nc.tensor.matmul(acc, weights[:, x, g, m * P:(m + 1) * P], moving[:, y, g, cols],
                                              start=(g, x, y) == (0, 0, 0), stop=(g, x, y) == (parts - 1, 0, 1))
                return op

            def h1_product(n):
                m, hb = n % (HID1 // P), n // (HID1 // P)
                split_product(h_ps(n), w1_hl, z_hl, ZGROUPS, m, slice(hb * 512, (hb + 1) * 512)).then_inc(h1_ps_ready, 1)

            pe.wait_ge(w_ready, ZGROUPS + 1)
            pe.wait_ge(z_ready, ZGROUPS)
            pe.wait_ge(prod_ready, BLOCKS * QUADS - 1)
            h1_product(0)
            add_up(BLOCKS - 1, QUADS - ZLAG)
            for n in range(1, 8):
                if n == 4:
                    pe.wait_ge(z_ready, ZGROUPS + 2)
                    pe.wait_ge(z_last_ready, 2)
                if n >= 4:
                    pe.wait_ge(h1_relu, n - 3)
                h1_product(n)
            n = 8
            for hb in range(2):
                pe.wait_ge(h1_ready, 4 * (hb + 1))
                for m in range(HID2 // P):
                    if n < 12:
                        pe.wait_ge(h1_relu, min(8, n - 3))
                    split_product(h_ps(n), w2_hl, h1_hl, HID1 // P, m, slice(hb * 512, (hb + 1) * 512)).then_inc(h2_ps_ready, 1)
                    n += 1
            pe.wait_ge(h2_ready, 4)
            for g in range(HID2 // P):
                for k in range(QUAD):
                    op = nc.tensor.matmul(y_ps(k), w3_sb[:, g:g + 1], h2T[:, g, k * BB:(k + 1) * BB],
                                          start=g == 0, stop=g == HID2 // P - 1)
            op.then_inc(y_ps_ready, 1)


def kernel(**inputs):
    import concourse.bacc as bacc
    from concourse.bass_utils import run_bass_kernel_spmd

    nc = bacc.Bacc("TRN2", target_bir_lowering=False, num_devices=1)
    arrays = {}

    def dram(name, a):
        a = np.ascontiguousarray(a)
        arrays[name] = a
        return nc.dram_tensor(name, a.shape, mybir.dt.from_np(a.dtype), kind="ExternalInput").ap()

    k_in = np.asarray(inputs["L0_rec_kernel"])
    w1_in = np.asarray(inputs["W_top1"])
    first = [r * (2 * FIELDS - r - 1) // 2 - r - 1 for r in range(FIELDS)]
    k_units = np.zeros((EMBED, len(UNITS), 2, EMBED), k_in.dtype)
    w1_rows = np.zeros((ZGROUPS, P, HID1), w1_in.dtype)
    spare = 0
    for n, (c, t) in enumerate(UNITS):
        for h in range(2):
            r = 2 * t + h
            if r < c:
                k_units[:, n, h] = k_in[:, first[r] + c]
                w1_rows[z_row(n, h)] = w1_in[first[r] + c]
            else:
                w1_rows[z_row(n, h)] = w1_in[PAIRS + spare]
                spare += 1
    kern = k_units.reshape(EMBED, KCHUNKS, 2, KHALF).transpose(1, 2, 0, 3).reshape(KCHUNKS, P, KHALF)
    ids = np.asarray(inputs["ids"]).reshape(BATCH // P, P, FIELDS).transpose(1, 0, 2).reshape(P, -1).view(np.uint32)

    args = [dram("ids", ids), [dram(f"tbl_{f}", np.asarray(inputs[f"tbl_{f}"])) for f in range(FIELDS)],
            dram("kern", kern), dram("dense", np.asarray(inputs["dense_ctx"]).T),
            dram("w1", w1_rows.transpose(1, 0, 2)), dram("b1", np.asarray(inputs["b_top1"]).reshape(-1, P).T),
            dram("w2", np.asarray(inputs["W_top2"]).reshape(-1, P, HID2).transpose(1, 0, 2)),
            dram("b2", np.asarray(inputs["b_top2"]).reshape(-1, P).T),
            dram("w3", np.asarray(inputs["W_top3"]).reshape(-1, P).T)]
    out = nc.dram_tensor("out", (1, BATCH), mybir.dt.float32, kind="ExternalOutput").ap()
    tower(nc, *args, out)
    r = run_bass_kernel_spmd(nc, [arrays], core_ids=[0])
    return r.results[0]["out"].reshape(BATCH, 1)
```
